# Optimizing a Trainium2 kernel written in Bass

```python
import numpy as np
import jax
import jax.numpy as jnp

def _softmax(x, axis=-1):
    return jax.nn.softmax(x, axis=axis)

def _gelu(x):
    return jax.nn.gelu(x, approximate=True)

def _silu(x):
    return jax.nn.silu(x)

def _sigmoid(x):
    return jax.nn.sigmoid(x)

def _layernorm(x, axis=-1, eps=1e-05):
    m = jnp.mean(x, axis=axis, keepdims=True)
    v = jnp.var(x, axis=axis, keepdims=True)
    return (x - m) / jnp.sqrt(v + eps)

def _scatter_add(tgt, idx, src, axis=0):
    return tgt.at[idx].add(src)

def _segment_sum(src, seg, n):
    return jax.ops.segment_sum(src, seg, n)
kernel_name = 'mk_dlrm_tower_d1_rec_r8_8ade28'

def setup_inputs(seed: int=0):
    np.random.seed(seed)
    _w = jnp.asarray

    def _rec_inputs():
        import jax
        import jax.numpy as jnp
        _tk = jax.random.key(seed)
        ids = jnp.stack([jax.random.randint(jax.random.fold_in(_tk, 200 + f), (2048,), 0, v, jnp.int32) for f, v in enumerate([1000, 1000, 1250, 12500, 1000, 12500, 125000, 12500, 1000, 1000, 12500, 12500, 1250, 1000, 1250, 1250, 1250, 1000, 1250, 12500, 1250, 1000, 1250, 1000, 12500, 1250])], axis=1)
        tbl_0 = 0.05 * jax.random.normal(jax.random.fold_in(_tk, 500 + 0), (1000, 128), jnp.float32)
        tbl_1 = 0.05 * jax.random.normal(jax.random.fold_in(_tk, 500 + 1), (1000, 128), jnp.float32)
        tbl_2 = 0.05 * jax.random.normal(jax.random.fold_in(_tk, 500 + 2), (1250, 128), jnp.float32)
        tbl_3 = 0.05 * jax.random.normal(jax.random.fold_in(_tk, 500 + 3), (12500, 128), jnp.float32)
        tbl_4 = 0.05 * jax.random.normal(jax.random.fold_in(_tk, 500 + 4), (1000, 128), jnp.float32)
        tbl_5 = 0.05 * jax.random.normal(jax.random.fold_in(_tk, 500 + 5), (12500, 128), jnp.float32)
        tbl_6 = 0.05 * jax.random.normal(jax.random.fold_in(_tk, 500 + 6), (125000, 128), jnp.float32)
        tbl_7 = 0.05 * jax.random.normal(jax.random.fold_in(_tk, 500 + 7), (12500, 128), jnp.float32)
        tbl_8 = 0.05 * jax.random.normal(jax.random.fold_in(_tk, 500 + 8), (1000, 128), jnp.float32)
        tbl_9 = 0.05 * jax.random.normal(jax.random.fold_in(_tk, 500 + 9), (1000, 128), jnp.float32)
        tbl_10 = 0.05 * jax.random.normal(jax.random.fold_in(_tk, 500 + 10), (12500, 128), jnp.float32)
        tbl_11 = 0.05 * jax.random.normal(jax.random.fold_in(_tk, 500 + 11), (12500, 128), jnp.float32)
        tbl_12 = 0.05 * jax.random.normal(jax.random.fold_in(_tk, 500 + 12), (1250, 128), jnp.float32)
        tbl_13 = 0.05 * jax.random.normal(jax.random.fold_in(_tk, 500 + 13), (1000, 128), jnp.float32)
        tbl_14 = 0.05 * jax.random.normal(jax.random.fold_in(_tk, 500 + 14), (1250, 128), jnp.float32)
        tbl_15 = 0.05 * jax.random.normal(jax.random.fold_in(_tk, 500 + 15), (1250, 128), jnp.float32)
        tbl_16 = 0.05 * jax.random.normal(jax.random.fold_in(_tk, 500 + 16), (1250, 128), jnp.float32)
        tbl_17 = 0.05 * jax.random.normal(jax.random.fold_in(_tk, 500 + 17), (1000, 128), jnp.float32)
        tbl_18 = 0.05 * jax.random.normal(jax.random.fold_in(_tk, 500 + 18), (1250, 128), jnp.float32)
        tbl_19 = 0.05 * jax.random.normal(jax.random.fold_in(_tk, 500 + 19), (12500, 128), jnp.float32)
        tbl_20 = 0.05 * jax.random.normal(jax.random.fold_in(_tk, 500 + 20), (1250, 128), jnp.float32)
        tbl_21 = 0.05 * jax.random.normal(jax.random.fold_in(_tk, 500 + 21), (1000, 128), jnp.float32)
        tbl_22 = 0.05 * jax.random.normal(jax.random.fold_in(_tk, 500 + 22), (1250, 128), jnp.float32)
        tbl_23 = 0.05 * jax.random.normal(jax.random.fold_in(_tk, 500 + 23), (1000, 128), jnp.float32)
        tbl_24 = 0.05 * jax.random.normal(jax.random.fold_in(_tk, 500 + 24), (12500, 128), jnp.float32)
        tbl_25 = 0.05 * jax.random.normal(jax.random.fold_in(_tk, 500 + 25), (1250, 128), jnp.float32)
        _rk = jax.random.fold_in(_tk, 7)
        r_dense_x = -0.000514642 + 1.00011 * jax.random.normal(jax.random.fold_in(_rk, 101), (2048, 128), jnp.float32)
        W_top1 = 0.0456912 * jax.random.normal(jax.random.fold_in(_tk, 801), (479, 512), jnp.float32)
        W_top2 = 0.0441942 * jax.random.normal(jax.random.fold_in(_tk, 802), (512, 256), jnp.float32)
        W_top3 = 0.0625 * jax.random.normal(jax.random.fold_in(_tk, 803), (256, 1), jnp.float32)
        b_top1 = jnp.zeros((512,), jnp.float32)
        b_top2 = jnp.zeros((256,), jnp.float32)
        return (r_dense_x, ids, tbl_0, tbl_1, tbl_2, tbl_3, tbl_4, tbl_5, tbl_6, tbl_7, tbl_8, tbl_9, tbl_10, tbl_11, tbl_12, tbl_13, tbl_14, tbl_15, tbl_16, tbl_17, tbl_18, tbl_19, tbl_20, tbl_21, tbl_22, tbl_23, tbl_24, tbl_25, W_top1, b_top1, W_top2, b_top2, W_top3)
    r_dense_x, ids, tbl_0, tbl_1, tbl_2, tbl_3, tbl_4, tbl_5, tbl_6, tbl_7, tbl_8, tbl_9, tbl_10, tbl_11, tbl_12, tbl_13, tbl_14, tbl_15, tbl_16, tbl_17, tbl_18, tbl_19, tbl_20, tbl_21, tbl_22, tbl_23, tbl_24, tbl_25, W_top1, b_top1, W_top2, b_top2, W_top3 = _rec_inputs()

    def _L0_rec_setup():
        import jax, jax.numpy as jnp
        import numpy as np
        F = 26
        D = 128
        B = 2048
        _TRIU_I, _TRIU_J = np.triu_indices(F + 1, k=1)
        _TRIU_I = jnp.asarray(_TRIU_I)
        _TRIU_J = jnp.asarray(_TRIU_J)
        key = jax.random.key(seed)
        k1, k2 = jax.random.split(key)
        sparse_x = jax.random.normal(k1, (B, F, D), dtype=jnp.float32)
        dense_x = jax.random.normal(k2, (B, D), dtype=jnp.float32)
        return {'sparse_x': sparse_x, 'dense_x': dense_x}
    _L0_rec_all = _L0_rec_setup()
    _L0_rec_in = {k: v for k, v in _L0_rec_all.items() if k in ()}
    del _L0_rec_all
    return {'r_dense_x': r_dense_x, 'ids': ids, 'tbl_0': tbl_0, 'tbl_1': tbl_1, 'tbl_2': tbl_2, 'tbl_3': tbl_3, 'tbl_4': tbl_4, 'tbl_5': tbl_5, 'tbl_6': tbl_6, 'tbl_7': tbl_7, 'tbl_8': tbl_8, 'tbl_9': tbl_9, 'tbl_10': tbl_10, 'tbl_11': tbl_11, 'tbl_12': tbl_12, 'tbl_13': tbl_13, 'tbl_14': tbl_14, 'tbl_15': tbl_15, 'tbl_16': tbl_16, 'tbl_17': tbl_17, 'tbl_18': tbl_18, 'tbl_19': tbl_19, 'tbl_20': tbl_20, 'tbl_21': tbl_21, 'tbl_22': tbl_22, 'tbl_23': tbl_23, 'tbl_24': tbl_24, 'tbl_25': tbl_25, 'W_top1': W_top1, 'b_top1': b_top1, 'W_top2': W_top2, 'b_top2': b_top2, 'W_top3': W_top3}

def reference(r_dense_x, ids, tbl_0, tbl_1, tbl_2, tbl_3, tbl_4, tbl_5, tbl_6, tbl_7, tbl_8, tbl_9, tbl_10, tbl_11, tbl_12, tbl_13, tbl_14, tbl_15, tbl_16, tbl_17, tbl_18, tbl_19, tbl_20, tbl_21, tbl_22, tbl_23, tbl_24, tbl_25, W_top1, b_top1, W_top2, b_top2, W_top3):
    import jax
    import jax.numpy as jnp

    def _L0_rec_ref(sparse_x, dense_x):
        import jax, jax.numpy as jnp
        import numpy as np
        F = 26
        D = 128
        B = 2048
        _TRIU_I, _TRIU_J = np.triu_indices(F + 1, k=1)
        _TRIU_I = jnp.asarray(_TRIU_I)
        _TRIU_J = jnp.asarray(_TRIU_J)
        combined = jnp.concatenate([sparse_x, dense_x[:, None, :]], axis=1)
        interact = jnp.einsum('bfd,bgd->bfg', combined, combined)
        return interact[:, _TRIU_I, _TRIU_J]
    e = jnp.stack([tbl_0[ids[:, 0]], tbl_1[ids[:, 1]], tbl_2[ids[:, 2]], tbl_3[ids[:, 3]], tbl_4[ids[:, 4]], tbl_5[ids[:, 5]], tbl_6[ids[:, 6]], tbl_7[ids[:, 7]], tbl_8[ids[:, 8]], tbl_9[ids[:, 9]], tbl_10[ids[:, 10]], tbl_11[ids[:, 11]], tbl_12[ids[:, 12]], tbl_13[ids[:, 13]], tbl_14[ids[:, 14]], tbl_15[ids[:, 15]], tbl_16[ids[:, 16]], tbl_17[ids[:, 17]], tbl_18[ids[:, 18]], tbl_19[ids[:, 19]], tbl_20[ids[:, 20]], tbl_21[ids[:, 21]], tbl_22[ids[:, 22]], tbl_23[ids[:, 23]], tbl_24[ids[:, 24]], tbl_25[ids[:, 25]]], axis=1)
    z = _L0_rec_ref(e, r_dense_x)
    z = z.reshape(z.shape[0], -1)
    h = jnp.concatenate([z, r_dense_x], axis=1)
    h = jnp.maximum(h @ W_top1 + b_top1, 0.0)
    h = jnp.maximum(h @ W_top2 + b_top2, 0.0)
    y = h @ W_top3
    return y

_drawn_inputs = setup_inputs


def setup_inputs(seed=0):
    import zlib

    import numpy as np

    out = dict(_drawn_inputs(seed))
    spreads = {'b_top1': (0.0, 0.1), 'b_top2': (0.0, 0.1)}
    factors = {}
    for name, (base, spread) in spreads.items():
        noise = np.random.default_rng([zlib.crc32(name.encode()), seed]).standard_normal(out[name].shape)
        drawn = base * np.exp(spread * noise) if base else spread * noise
        out[name] = jnp.asarray(drawn.astype(out[name].dtype))
    for name, factor in factors.items():
        out[name] = (out[name] * factor).astype(out[name].dtype)
    return out
```

```python
from contextlib import ExitStack

import numpy as np

import concourse.bass as bass
from concourse import mybir

F32 = mybir.dt.float32
F32R = mybir.dt.float32r
F16 = mybir.dt.float16
I32 = mybir.dt.int32
ALU = mybir.AluOpType
ACT = mybir.ActivationFunctionType

P = 128
BATCH = 2048
DIM = 128
TABLES = 26
NF = TABLES + 1
QUARTERS = 4
TILES = 4
QCOLS = TILES * P
HID1, HID2 = 512, 256

ONE_HOT = [0, 1, 4, 8, 9, 13]
ONE_HOT_ROWS = 1000
GATHERED = [f for f in range(TABLES) if f not in ONE_HOT]
FEATURES = ONE_HOT + GATHERED + [TABLES]
NO = len(ONE_HOT)
NG = len(GATHERED)
SLOTS = NG + 1
CHUNKS = 8
CROWS = ONE_HOT_ROWS // CHUNKS
OH_BUFS = 3

SBLK = 4
GROUPS = P // SBLK
T_UNITS = [(a, min(8, SLOTS - a)) for a in range(0, SLOTS, 8)]
G_UNITS = 4
G_PER_UNIT = GROUPS // G_UNITS
UNITS = len(T_UNITS) + G_UNITS
HALF_G = 2 * GROUPS
NK = (NF - 1) // 2
ZCOLS = NF + NK
IROWS = 9
PCHUNK = IROWS * NK
PCHUNKS = NF // IROWS
MLP_USES = HID1 // P + HID2 // P + 1
SPREAD = (1, 2, 3)
PER_STEP = NO * CHUNKS // len(SPREAD)
FPAD = 32


def pair_rows():
    rows = []
    for i in range(NF):
        for k in range(1, NK + 1):
            a, b = sorted((FEATURES[i], FEATURES[(i + k) % NF]))
            rows.append(a * (NF - 1) - a * (a - 1) // 2 + b - a - 1)
    return np.array(rows + list(range(len(rows), len(rows) + DIM)))


def dlrm(nc, dense, ids, ids_rows, tables, w1, b1, w2, b2, w3, out):
    with ExitStack() as ctx:
        def sb(name, shape, dt=F32):
            return ctx.enter_context(nc.sbuf_tensor(name, shape, dt))

        def ps(name, shape):
            return ctx.enter_context(nc.psum_tensor(name, shape, F32))

        def sem(name):
            return ctx.enter_context(nc.semaphore(name))

        tab_hi = sb("tab_hi", [P, NO, CHUNKS, DIM], F32R)
        tab_lo = sb("tab_lo", [P, NO, CHUNKS, DIM], F32R)
        looked_up = sb("looked_up", [P, 2, NO, QCOLS])
        rows = sb("rows", [P, TILES, SLOTS, DIM])
        ct = sb("ct", [P, 2, GROUPS, SBLK, FPAD])
        z = sb("z", [P, 2, NF, HALF_G])
        pairs = sb("pairs", [PCHUNK, PCHUNKS, QCOLS])
        dense_t = sb("dense_t", [P, 2, QCOLS])
        h1 = sb("h1", [P, HID1 // P, QCOLS])
        h2 = sb("h2", [P, HID2 // P, QCOLS])
        w1_sb = sb("w1_sb", [P, PCHUNKS + 1, HID1])
        w2_sb = sb("w2_sb", [P, HID1 // P, HID2])
        w3_sb = sb("w3_sb", [P, HID2 // P])
        b1_sb = sb("b1_sb", [P, HID1 // P])
        b2_sb = sb("b2_sb", [P, HID2 // P])
        one_hot = sb("one_hot", [CROWS, OH_BUFS, QCOLS], F32R)
        small = sb("small", [33, BATCH // 2])
        ids16 = small[0:NO, :].bitcast(F16)
        y = small[32:33, 0:QCOLS]
        pick = sb("pick", [NO, NO, CROWS], F16)
        row_no_i = sb("row_no_i", [P, CHUNKS], I32)
        row_no = sb("row_no", [P, CHUNKS])
        ident = sb("ident", [P, P])
        idx = sb("idx", [P, TILES, TABLES], I32)
        raw = h1[:].rearrange("p m n -> p (m n)").rearrange("p (r n) -> p r n", r=2)
        ids_int = ct[0:NO, 0].rearrange("p g s f -> p (g s f)")[:, 0:BATCH].bitcast(I32)

        ring = [ps(f"ring{r}", [P, 2, 512]) for r in range(2)]
        spread_ids = ps("spread_ids", [P, 512])
        table_out = ps("table_out", [P, 512])
        mlp = [ps(f"mlp{r}", [P, 512]) for r in range(2)]

        z_dram = nc.dram_tensor("z_dram", [2, SBLK, 32, ZCOLS, HALF_G], F32, kind="Internal").ap()

        idx_loaded = [sem(f"idx_loaded{t}") for t in range(TILES)]
        dense_loaded = [sem(f"dense_loaded{t}") for t in range(TILES)]
        gathered = [sem(f"gathered{t}") for t in range(TILES)]
        ids_loaded = sem("ids_loaded")
        ids_converted = sem("ids_converted")
        raw_loaded = [sem(f"raw_loaded{r}") for r in range(2)]
        hi_made = sem("hi_made")
        lo_made = sem("lo_made")
        cleared = sem("cleared")
        consts_made = sem("consts_made")
        row_no_made = sem("row_no_made")
        padding_made = sem("padding_made")
        weights_loaded = sem("weights_loaded")
        ids_spread = sem("ids_spread")
        one_hot_made = sem("one_hot_made")
        one_hot_used = sem("one_hot_used")
        table_read = sem("table_read")
        placed = sem("placed")
        ring_filled = sem("ring_filled")
        ring_read_act = sem("ring_read_act")
        ring_read_dve = sem("ring_read_dve")
        z_stored = [sem(f"z_stored{h}") for h in range(2)]
        pairs_loaded = [sem(f"pairs_loaded{h}") for h in range(2)]
        mlp_filled = sem("mlp_filled")
        mlp_read = sem("mlp_read")
        y_stored = sem("y_stored")
        settled = sem("settled")

        block = ctx.enter_context(nc.Block())

        def settle(eng):
            eng.sem_inc(settled, 1)

        def rows_read(q, t):
            return UNITS * (q * TILES + t) + len(T_UNITS)

        def table_rows(f):
            return tables[f].rearrange("(p c) d -> p (c d)", c=CHUNKS)

        def gram_view(r, s):
            return ring[r][32 * s:32 * s + NF, :, 0:4 * SBLK * NF].rearrange(
                "p b (g s f) -> p b g s f", g=4, s=SBLK)[:, :, :, s, :]

        def z_view(t, gu, s):
            at = (t % 2) * GROUPS + gu * G_PER_UNIT
            return z[32 * s:32 * s + NF, t // 2, :, at:at + G_PER_UNIT].rearrange(
                "p f (b g) -> p b g f", b=2)

        @block.sync
        def _(sp):
            def load_idx(q, t):
                sp.dma_start(idx[:, t, :], ids[bass.ds((q * TILES + t) * P, P), :]).then_inc(idx_loaded[t], 16)

            def load_dense(q, t):
                sp.dma_start(rows[:, t, NG, :], dense[bass.ds((q * TILES + t) * P, P), :]).then_inc(
                    dense_loaded[t], 16)

            def load_next(q, t):
                sp.wait_ge(gathered[t], 16 * NG * (q + 1))
                settle(sp)
                load_idx(q + 1, t)
                sp.wait_ge(ring_filled, rows_read(q, t))
                settle(sp)
                load_dense(q + 1, t)

            def regroup(q, t):
                h = t // 2
                sp.wait_ge(ring_read_act, UNITS * (q * TILES + t + 1))
                settle(sp)
                sp.wait_ge(ring_read_dve, G_UNITS * (q * TILES + t + 1))
                settle(sp)
                sp.wait_ge(mlp_filled, MLP_USES * q + 1)
                settle(sp)
                dst = z_dram[h].rearrange("s i j g -> (s i) j g")
                sp.dma_start(dst[:, 0:NF, :], z[:, h, :, :]).then_inc(z_stored[h], 16)
                sp.dma_start(dst[:, NF:ZCOLS, :], z[:, h, 0:NK, :]).then_inc(z_stored[h], 16)
                sp.wait_ge(z_stored[h], 32 * (q + 2))
                settle(sp)
                for c in range(PCHUNKS):
                    for s in range(SBLK):
                        src = bass.AP(z_dram.tensor, z_dram[h, s, c * IROWS, c * IROWS + 1, 0:1].offset,
                                      [[(ZCOLS + 1) * HALF_G, IROWS], [HALF_G, NK], [1, HALF_G]])
                        at = (h * SBLK + s) * HALF_G
                        sp.dma_start(pairs[:, c, at:at + HALF_G], src).then_inc(pairs_loaded[h], 16)

            def store_y(q):
                sp.wait_ge(mlp_read, MLP_USES * (q + 1) + 1)
                settle(sp)
                for h in range(2):
                    n = QCOLS // 2
                    dst = out[bass.ds(q * QCOLS + h * n, n), :].rearrange(
                        "(t s g) o -> o s t g", t=2, s=SBLK)
                    sp.dma_start(dst, y[:, h * n:(h + 1) * n].rearrange(
                        "o (s t g) -> o s t g", s=SBLK, t=2)).then_inc(y_stored, 16)

            sp.sem_inc(y_stored, 32)
            for h in range(2):
                sp.sem_inc(z_stored[h], 32)
            load_idx(0, 0)
            sp.dma_start(ids_int, ids_rows).then_inc(ids_loaded, 16)
            for t in range(1, TILES):
                load_idx(0, t)
            for k, f in enumerate(ONE_HOT):
                if k == 2:
                    for t in range(TILES):
                        load_dense(0, t)
                if k >= 2:
                    sp.wait_ge(lo_made, k - 1)
                sp.dma_start(raw[0:CROWS, k % 2, :], table_rows(f)).then_inc(raw_loaded[k % 2], 16)
            for dst, src in (
                (w1_sb[0:PCHUNK, 0:PCHUNKS, :], w1[0:PCHUNK * PCHUNKS, :].rearrange("(c p) n -> p c n", p=PCHUNK)),
                (w1_sb[:, PCHUNKS, :], w1[PCHUNK * PCHUNKS:PCHUNK * PCHUNKS + DIM, :]),
                (w2_sb[:], w2.rearrange("(c p) n -> p c n", p=P)),
                (w3_sb[:], w3),
                (b1_sb[:], b1),
                (b2_sb[:], b2),
            ):
                sp.dma_start(dst, src).then_inc(weights_loaded, 16)

            sp.wait_ge(padding_made, 2)
            with sp.Fori(0, QUARTERS - 1) as q:
                for t in range(TILES):
                    load_next(q, t)
                    if t % 2:
                        regroup(q, t)
                store_y(q)
            for t in range(1, TILES, 2):
                regroup(QUARTERS - 1, t)
            store_y(QUARTERS - 1)
            sp.wait_ge(y_stored, 32 * (QUARTERS + 1))

        @block.gpsimd
        def _(pool):
            pool.memset(ident[:], 0.0).then_inc(cleared, 1)
            pool.memset(pick[:], 0.0).then_inc(cleared, 1)
            pool.iota(row_no_i[:], [[1, CHUNKS]], base=0, channel_multiplier=CHUNKS).then_inc(consts_made, 1)
            pool.wait_ge(cleared, 2)
            pool.affine_select(out=ident[:], in_=ident[:], compare_op=ALU.not_equal, fill=1.0, base=0,
                               pattern=[[-1, P]], channel_multiplier=1).then_inc(consts_made, 1)
            pool.affine_select(out=pick[:], in_=pick[:], compare_op=ALU.not_equal, fill=1.0, base=0,
                               pattern=[[-1, NO], [0, CROWS]], channel_multiplier=1).then_inc(consts_made, 1)

            def gather(t):
                for s, f in enumerate(GATHERED):
                    pool.indirect_dma_start(
                        rows[:, t, s, :], None, tables[f],
                        bass.IndirectOffsetOnAxis(ap=idx[:, t, f:f + 1], axis=0)).then_inc(gathered[t], 16)

            for t in range(TILES):
                pool.wait_ge(idx_loaded[t], 16)
                gather(t)
            with pool.Fori(1, QUARTERS) as q:
                for t in range(TILES):
                    pool.wait_ge(ring_filled, rows_read(q - 1, t))
                    pool.wait_ge(idx_loaded[t], 16 * (q + 1))
                    settle(pool)
                    gather(t)

        @block.tensor
        def _(pe):
            def spread(q, k):
                pe.wait_ge(one_hot_made, CHUNKS * (q * NO + k))
                settle(pe)
                pe.matmul(spread_ids[0:CROWS, :], pick[:, k, :], ids16[:, bass.ds(q * QCOLS, QCOLS)],
                          start=True, stop=True).then_inc(ids_spread, 1)

            def look_up(q, k, c):
                if c == CHUNKS - 2 and k + 1 < NO:
                    spread(q, k + 1)
                pe.wait_ge(one_hot_made, CHUNKS * (q * NO + k) + c + 1)
                if c == 0:
                    pe.wait_ge(table_read, q * NO + k)
                hot = one_hot[:, (k * CHUNKS + c) % OH_BUFS, :]
                pe.matmul(table_out[:], tab_hi[0:CROWS, k, c, :], hot, start=(c == 0), stop=False)
                pe.matmul(table_out[:], tab_lo[0:CROWS, k, c, :], hot, start=False,
                          stop=(c == CHUNKS - 1)).then_inc(one_hot_used, 1)

            def ring_free(q, t, u):
                w = UNITS * (q * TILES + t) + u
                if isinstance(w, int) and w < 2:
                    return
                pe.wait_ge(ring_read_act, w - 1)
                g = u - 2 - len(T_UNITS)
                if g >= 0:
                    pe.wait_ge(ring_read_dve, G_UNITS * (q * TILES + t) + g + 1)
                elif u < 2:
                    pe.wait_ge(ring_read_dve, G_UNITS * (q * TILES + t) + u - 1)

            def tile(q, t, chunks):
                if chunks and chunks[0] == 0:
                    spread(q + 1, 0)
                pe.wait_ge(gathered[t], 16 * NG * (q + 1))
                pe.wait_ge(dense_loaded[t], 16 * (q + 1))
                for u, (first, n) in enumerate(T_UNITS):
                    r = (UNITS * t + u) % 2
                    ring_free(q, t, u)
                    for i in range(n):
                        mm = pe.transpose(ring[r][:, i // 4, (i % 4) * P:(i % 4 + 1) * P],
                                          rows[:, t, first + i, :], ident[:])
                    mm.then_inc(ring_filled, 1)
                done = 0
                for gu in range(G_UNITS):
                    u = len(T_UNITS) + gu
                    r = (UNITS * t + u) % 2
                    if gu == 0:
                        pe.wait_ge(placed, q * TILES + t + 1)
                        pe.wait_ge(ring_read_act, UNITS * (q * TILES + t) + len(T_UNITS))
                    ring_free(q, t, u)
                    for i in range(G_PER_UNIT):
                        g = gu * G_PER_UNIT + i
                        left = ct[:, t % 2, g].rearrange("p s f -> p (s f)")
                        right = ct[:, t % 2, g, :, 0:NF]
                        n = SBLK * NF
                        mm = pe.matmul(ring[r][:, i // 4, (i % 4) * n:(i % 4 + 1) * n], left, right,
                                       start=True, stop=True)
                        if i == G_PER_UNIT - 1:
                            mm.then_inc(ring_filled, 1)
                        while chunks and done < (g + 1) * len(chunks) // GROUPS:
                            look_up(q + 1, *divmod(chunks[done], CHUNKS))
                            done += 1

            def mlp_layers(q):
                def bank(j):
                    pe.wait_ge(mlp_read, MLP_USES * q + max(j, 1))
                    return mlp[j % 2]

                n1, n2 = HID1 // P, HID2 // P
                for h in range(2):
                    pe.wait_ge(pairs_loaded[h], 16 * PCHUNKS * SBLK * (q + 1))
                for m in range(n1):
                    acc = bank(m)
                    cols = slice(m * P, (m + 1) * P)
                    for c in range(PCHUNKS):
                        pe.matmul(acc[:], w1_sb[0:PCHUNK, c, cols], pairs[:, c, :], start=(c == 0), stop=False)
                    pe.matmul(acc[:], w1_sb[:, PCHUNKS, cols], dense_t[:, q % 2, :],
                              start=False, stop=True).then_inc(mlp_filled, 1)
                for m in range(n2):
                    acc = bank(n1 + m)
                    pe.wait_ge(mlp_read, MLP_USES * q + n1 + 1)
                    for c in range(n1):
                        mm = pe.matmul(acc[:], w2_sb[:, c, m * P:(m + 1) * P], h1[:, c, :],
                                       start=(c == 0), stop=(c == n1 - 1))
                    mm.then_inc(mlp_filled, 1)
                acc = bank(n1 + n2)
                pe.wait_ge(mlp_read, MLP_USES * q + n1 + n2 + 1)
                for c in range(n2):
                    mm = pe.matmul(acc[0:1, :], w3_sb[:, c:c + 1], h2[:, c, :], start=(c == 0), stop=(c == n2 - 1))
                mm.then_inc(mlp_filled, 1)

            pe.sem_inc(mlp_filled, 1)
            pe.wait_ge(consts_made, 3)
            pe.wait_ge(ids_converted, 1)
            spread(0, 0)
            for k in range(NO):
                pe.wait_ge(lo_made, k + 1)
                for c in range(CHUNKS):
                    look_up(0, k, c)
            pe.wait_ge(padding_made, 2)
            tile(0, 0, [])
            pe.wait_ge(weights_loaded, 16 * 6)
            with pe.Fori(0, QUARTERS - 1) as q:
                for t in range(1, TILES):
                    tile(q, t, list(range(PER_STEP * (t - 1), PER_STEP * t)))
                tile(q + 1, 0, [])
                mlp_layers(q)
            for t in range(1, TILES):
                tile(QUARTERS - 1, t, [])
            mlp_layers(QUARTERS - 1)

        @block.scalar
        def _(act):
            def read_table(q, k):
                act.wait_ge(one_hot_used, CHUNKS * (q * NO + k + 1))
                settle(act)
                act.copy(looked_up[:, q % 2, k, :], table_out[:]).then_inc(table_read, 1)

            def tile(q, t, chunks):
                slot = ct[:, t % 2].rearrange("p g s f -> p f s g")
                act.wait_ge(table_read, NO * (q + 1))
                if not (isinstance(q, int) and q == 0 and t < 2):
                    act.wait_ge(ring_filled, UNITS * (q * TILES + t - 1))
                settle(act)
                for k in range(NO):
                    cp = act.copy(slot[:, k], looked_up[:, q % 2, k, t * P:(t + 1) * P].rearrange(
                        "p (s g) -> p s g", s=SBLK))
                cp.then_inc(placed, 1)
                for u, (first, n) in enumerate(T_UNITS):
                    r = (UNITS * t + u) % 2
                    act.wait_ge(ring_filled, UNITS * (q * TILES + t) + u + 1)
                    settle(act)
                    src = ring[r][:].rearrange("p b n -> p (b n)")
                    if first + n == SLOTS:
                        d = dense_t[:, q % 2, :].rearrange("p (h s t g) -> p h s t g", h=2, s=SBLK, t=2)
                        act.copy(d[:, t // 2, :, t % 2, :],
                                 src[:, (n - 1) * P:n * P].rearrange("p (s g) -> p s g", s=SBLK))
                    act.copy(slot[:, NO + first:NO + first + n],
                             src[:, 0:n * P].rearrange("p (k s g) -> p k s g", k=n, s=SBLK)).then_inc(
                                 ring_read_act, 1)
                for gu in range(G_UNITS):
                    u = len(T_UNITS) + gu
                    act.wait_ge(ring_filled, UNITS * (q * TILES + t) + u + 1)
                    if gu == 0 and t % 2 == 0:
                        act.wait_ge(z_stored[t // 2], 32 * (q + 1))
                    act.copy(z_view(t, gu, 0), gram_view((UNITS * t + u) % 2, 0))
                    act.copy(z_view(t, gu, 1), gram_view((UNITS * t + u) % 2, 1)).then_inc(ring_read_act, 1)
                    if chunks and gu % 2:
                        read_table(q + 1, chunks[gu * PER_STEP // G_UNITS] // CHUNKS)

            def mlp_layers(q):
                n1, n2 = HID1 // P, HID2 // P
                for j in range(n1 + n2):
                    act.wait_ge(mlp_filled, MLP_USES * q + j + 2)
                    dst, bias = (h1[:, j, :], b1_sb[:, j:j + 1]) if j < n1 else (h2[:, j - n1, :],
                                                                                 b2_sb[:, j - n1:j - n1 + 1])
                    act.activation(dst, mlp[j % 2][:], ACT.Relu, bias=bias).then_inc(mlp_read, 1)
                act.wait_ge(mlp_filled, MLP_USES * (q + 1) + 1)
                act.wait_ge(y_stored, 32 * (q + 1))
                act.copy(y, mlp[(n1 + n2) % 2][0:1, :]).then_inc(mlp_read, 1)

            act.sem_inc(mlp_read, 1)
            for k in range(NO):
                act.wait_ge(raw_loaded[k % 2], 16 * (k // 2 + 1))
                act.copy(tab_hi[0:CROWS, k].rearrange("p c d -> p (c d)"), raw[0:CROWS, k % 2, :]).then_inc(
                    hi_made, 1)
                if k >= 1:
                    read_table(0, k - 1)
            read_table(0, NO - 1)
            act.wait_ge(padding_made, 2)
            tile(0, 0, [])
            act.wait_ge(weights_loaded, 16 * 6)
            with act.Fori(0, QUARTERS - 1) as q:
                for t in range(1, TILES):
                    tile(q, t, list(range(PER_STEP * (t - 1), PER_STEP * t)))
                tile(q + 1, 0, [])
                mlp_layers(q)
            for t in range(1, TILES):
                tile(QUARTERS - 1, t, [])
            mlp_layers(QUARTERS - 1)

        @block.vector
        def _(dve):
            def compare(q, k, c):
                if c == 0:
                    dve.wait_ge(ids_spread, q * NO + k + 1)
                if not (isinstance(q, int) and q * NO + k == 0 and c < OH_BUFS):
                    dve.wait_ge(one_hot_used, CHUNKS * (q * NO + k) + c - OH_BUFS + 1)
                dve.tensor_scalar(one_hot[:, (k * CHUNKS + c) % OH_BUFS, :], spread_ids[0:CROWS, :], row_no[0:CROWS, c:c + 1],
                                  None, ALU.is_equal).then_inc(one_hot_made, 1)

            def read_unit(q, t, gu):
                u = len(T_UNITS) + gu
                dve.wait_ge(ring_filled, UNITS * (q * TILES + t) + u + 1)
                if gu == 0 and t % 2 == 0:
                    dve.wait_ge(z_stored[t // 2], 32 * (q + 1))
                dve.tensor_copy(z_view(t, gu, 2), gram_view((UNITS * t + u) % 2, 2))
                dve.tensor_copy(z_view(t, gu, 3), gram_view((UNITS * t + u) % 2, 3)).then_inc(ring_read_dve, 1)

            def tile(q, t, chunks):
                per = len(chunks) // G_UNITS
                for n, chunk in enumerate(chunks):
                    compare(q + 1, *divmod(chunk, CHUNKS))
                    gu = (n - per - 2) // per
                    if n == per * (gu + 1) + 2 and 0 <= gu < G_UNITS - 1:
                        read_unit(q, t, gu)
                for gu in range(G_UNITS - 1 if chunks else 0, G_UNITS):
                    read_unit(q, t, gu)

            dve.wait_ge(consts_made, 3)
            dve.tensor_copy(row_no[:], row_no_i[:]).then_inc(row_no_made, 1)
            dve.wait_ge(ids_loaded, 16)
            dve.tensor_copy(ids16, ids_int).then_inc(ids_converted, 1)
            dve.wait_ge(row_no_made, 1)
            for k in range(NO):
                dve.wait_ge(hi_made, k + 1)
                dve.tensor_tensor(tab_lo[0:CROWS, k].rearrange("p c d -> p (c d)"), raw[0:CROWS, k % 2, :],
                                  tab_hi[0:CROWS, k].rearrange("p c d -> p (c d)").bitcast(F32),
                                  ALU.subtract).then_inc(lo_made, 1)
                for c in range(CHUNKS):
                    compare(0, k, c)
                if k == 0:
                    dve.memset(z[:], 0.0).then_inc(padding_made, 1)
                    dve.memset(ct[:, :, :, :, NF:FPAD], 0.0).then_inc(padding_made, 1)
            dve.wait_ge(padding_made, 2)
            tile(0, 0, [])
            with dve.Fori(0, QUARTERS - 1) as q:
                for t in range(1, TILES):
                    tile(q, t, list(range(PER_STEP * (t - 1), PER_STEP * t)))
                tile(q + 1, 0, [])
            for t in range(1, TILES):
                tile(QUARTERS - 1, t, [])


def kernel(**inputs):
    import concourse.bacc as bacc
    from concourse.bass_utils import run_bass_kernel_spmd

    nc = bacc.Bacc("TRN2", target_bir_lowering=False, num_devices=1)
    ids = np.asarray(inputs["ids"])
    arrays = {name: np.asarray(inputs[name]) for name in
              ["r_dense_x", "W_top2"] + [f"tbl_{f}" for f in range(TABLES)]}
    arrays["ids"] = ids
    arrays["ids_rows"] = ids.T[ONE_HOT]
    arrays["W_top1"] = np.asarray(inputs["W_top1"])[pair_rows()]
    for name in ("b_top1", "b_top2", "W_top3"):
        arrays[name] = np.asarray(inputs[name]).reshape(-1, P).T
    feed, aps = {}, {}
    for name, a in arrays.items():
        a = np.ascontiguousarray(a)
        feed[f"in_{name}"] = a
        aps[name] = nc.dram_tensor(f"in_{name}", a.shape, mybir.dt.from_np(a.dtype), kind="ExternalInput").ap()
    out = nc.dram_tensor("out", (BATCH, 1), F32, kind="ExternalOutput").ap()
    dlrm(nc, aps["r_dense_x"], aps["ids"], aps["ids_rows"], [aps[f"tbl_{f}"] for f in range(TABLES)],
         aps["W_top1"], aps["b_top1"], aps["W_top2"], aps["b_top2"], aps["W_top3"], out)
    return run_bass_kernel_spmd(nc, [feed], core_ids=[0]).results[0]["out"]
```

```python
from contextlib import ExitStack

import numpy as np

import concourse.bass as bass
from concourse import mybir

F32 = mybir.dt.float32
F32R = mybir.dt.float32r
F16 = mybir.dt.float16
I32 = mybir.dt.int32
ALU = mybir.AluOpType
ACT = mybir.ActivationFunctionType

P = 128
BATCH = 2048
DIM = 128
TABLES = 26
NF = TABLES + 1
QUARTERS = 4
TILES = 4
QCOLS = TILES * P
HID1, HID2 = 512, 256

ONE_HOT = [0, 1, 4, 8, 9, 13]
ONE_HOT_ROWS = 1000
GATHERED = [f for f in range(TABLES) if f not in ONE_HOT]
FEATURES = ONE_HOT + GATHERED + [TABLES]
NO = len(ONE_HOT)
NG = len(GATHERED)
CHUNKS = 8
CROWS = ONE_HOT_ROWS // CHUNKS
OH_BUFS = 3 if NO % 3 == 0 else 4
DVE_AHEAD = OH_BUFS - 1
RAW_BUFS = 3

SBLK = 4
GROUPS = P // SBLK
T_UNITS = [(a, min(8, NG - a)) for a in range(0, NG, 8)]
G_UNITS = 4
G_PER_UNIT = GROUPS // G_UNITS
UNITS = len(T_UNITS) + G_UNITS
HALF_G = 2 * GROUPS
NK = (NF - 1) // 2
ZCOLS = NF + NK
IROWS = 9
PCHUNK = IROWS * NK
PCHUNKS = NF // IROWS
HALF = QCOLS // 2
MLP_USES = HID1 // P + HID2 // P + 1
Z_STORES = 16 * 2 * SBLK
LEAD = 4
DVE_UNIT = 1


def chunks_in(t):
    return list(range(NO * CHUNKS * (t - 2) // 2, NO * CHUNKS * (t - 1) // 2))


def chunks_due(n, products):
    return LEAD + products * (n - LEAD) // GROUPS


def reads(tile, u):
    act = [v for v in range(u + 1) if v != DVE_UNIT]
    dve = [v for v in range(u + 1) if v == DVE_UNIT or v >= len(T_UNITS)]
    return (UNITS - 1) * tile + len(act), (G_UNITS + 1) * tile + len(dve)


FPAD = 32


def pair_rows():
    rows = []
    for i in range(NF):
        for k in range(1, NK + 1):
            a, b = sorted((FEATURES[i], FEATURES[(i + k) % NF]))
            rows.append(a * (NF - 1) - a * (a - 1) // 2 + b - a - 1)
    return np.array(rows + list(range(len(rows), len(rows) + DIM)))


def dlrm(nc, dense_cols, ids, ids_rows, tables, w1, b1, w2, b2, w3, out):
    with ExitStack() as ctx:
        def sb(name, shape, dt=F32):
            return ctx.enter_context(nc.sbuf_tensor(name, shape, dt))

        def ps(name, shape):
            return ctx.enter_context(nc.psum_tensor(name, shape, F32))

        def sem(name):
            return ctx.enter_context(nc.semaphore(name))

        tab_hi = sb("tab_hi", [P, NO, CHUNKS, DIM], F32R)
        tab_lo = sb("tab_lo", [P, NO, CHUNKS, DIM], F32R)
        looked_up = sb("looked_up", [P, 2, NO, QCOLS])
        rows = sb("rows", [P, TILES, NG, DIM])
        ct = sb("ct", [P, 2, GROUPS, SBLK, FPAD])
        z = sb("z", [P, 2, NF, HALF_G])
        pairs = sb("pairs", [PCHUNK, PCHUNKS, QCOLS])
        dense_t = sb("dense_t", [P, BATCH])
        h1 = sb("h1", [P, HID1 // P, HALF])
        h2 = sb("h2", [P, HID2 // P, HALF])
        w1_sb = sb("w1_sb", [P, PCHUNKS + 1, HID1])
        w2_sb = sb("w2_sb", [P, HID1 // P, HID2])
        w3_sb = sb("w3_sb", [P, HID2 // P])
        b1_sb = sb("b1_sb", [P, HID1 // P])
        b2_sb = sb("b2_sb", [P, HID2 // P])
        one_hot = sb("one_hot", [CROWS, OH_BUFS, QCOLS], F32R)
        small = sb("small", [33, BATCH // 2])
        ids16 = small[0:NO, :].bitcast(F16)
        y = small[32:33, 0:HALF]
        zero = sb("zero", [P, 1])
        pick = sb("pick", [NO, NO, CROWS], F16)
        row_no_i = sb("row_no_i", [P, CHUNKS], I32)
        row_no = sb("row_no", [P, CHUNKS])
        ident = sb("ident", [P, P])
        idx = sb("idx", [P, TILES, TABLES], I32)
        raw = z[:].rearrange("p h f g -> p (h f g)")[:, 0:RAW_BUFS * CHUNKS * DIM].rearrange(
            "p (r n) -> p r n", r=RAW_BUFS)
        ids_int = ct[0:NO, 0].rearrange("p g s f -> p (g s f)")[:, 0:BATCH].bitcast(I32)

        ring = [ps(f"ring{r}", [P, 2, 512]) for r in range(2)]
        spread_ids = ps("spread_ids", [P, 512])
        table_out = ps("table_out", [P, 512])
        mlp = [ps(f"mlp{r}", [P, 512]) for r in range(2)]

        z_dram = nc.dram_tensor("z_dram", [2, NF, ZCOLS, SBLK, HALF_G], F32, kind="Internal").ap()

        idx_loaded = [sem(f"idx_loaded{t}") for t in range(TILES)]
        dense_loaded = sem("dense_loaded")
        gathered = [sem(f"gathered{t}") for t in range(TILES)]
        ids_loaded = sem("ids_loaded")
        ids_converted = sem("ids_converted")
        raw_loaded = [sem(f"raw_loaded{r}") for r in range(RAW_BUFS)]
        hi_made = sem("hi_made")
        lo_made = sem("lo_made")
        cleared = sem("cleared")
        consts_made = sem("consts_made")
        row_no_made = sem("row_no_made")
        zero_made = sem("zero_made")
        padding_made = sem("padding_made")
        weights_loaded = sem("weights_loaded")
        ids_spread = sem("ids_spread")
        one_hot_made = sem("one_hot_made")
        one_hot_used = sem("one_hot_used")
        table_read = sem("table_read")
        placed = sem("placed")
        ring_filled = sem("ring_filled")
        ring_read_act = sem("ring_read_act")
        ring_read_dve = sem("ring_read_dve")
        z_stored = [sem(f"z_stored{h}") for h in range(2)]
        pairs_loaded = [sem(f"pairs_loaded{h}") for h in range(2)]
        mlp_filled = sem("mlp_filled")
        mlp_read = sem("mlp_read")
        y_stored = sem("y_stored")
        settled = sem("settled")

        block = ctx.enter_context(nc.Block())

        def settle(eng):
            eng.sem_inc(settled, 1)

        def rows_read(q, t):
            return UNITS * (q * TILES + t) + len(T_UNITS)

        def table_rows(f):
            return tables[f].rearrange("(p c) d -> p (c d)", c=CHUNKS)

        def issued_before(n, chunks):
            return min(p for p in range(GROUPS + 1) if chunks_due(len(chunks), p) > n)

        def transposed_unit(t, u):
            first, n = T_UNITS[u]
            dst = ct[:, t % 2].rearrange("p g s f -> p f s g")[:, NO + first:NO + first + n]
            src = ring[(UNITS * t + u) % 2][:].rearrange("p b n -> p (b n)")[:, 0:n * P]
            return dst, src.rearrange("p (k s g) -> p k s g", k=n, s=SBLK)

        def gram_view(r, s):
            return ring[r][32 * s:32 * s + NF, :, 0:4 * SBLK * NF].rearrange(
                "p b (g s f) -> p b g s f", g=4, s=SBLK)[:, :, :, s, :]

        def z_view(t, gu, s):
            at = (t % 2) * GROUPS + gu * G_PER_UNIT
            return z[32 * s:32 * s + NF, t // 2, :, at:at + G_PER_UNIT].rearrange(
                "p f (b g) -> p b g f", b=2)

        @block.sync
        def _(sp):
            def regroup(q, t):
                h = t // 2
                by_act, by_dve = reads(q * TILES + t, UNITS - 1)
                sp.wait_ge(mlp_filled, MLP_USES * (2 * q + h) + 1)
                settle(sp)
                for s in range(SBLK):
                    if s == 0:
                        sp.wait_ge(ring_read_act, by_act)
                        settle(sp)
                    if s == SBLK // 2:
                        sp.wait_ge(ring_read_dve, by_dve)
                        settle(sp)
                    block = z[32 * s:32 * s + NF, h, :, :]
                    dst = z_dram[h, :, :, s, :]
                    sp.dma_start(dst[:, 0:NF, :], block).then_inc(z_stored[h], 16)
                    sp.dma_start(dst[:, NF:ZCOLS, :], block[:, 0:NK, :]).then_inc(z_stored[h], 16)
                sp.wait_ge(z_stored[h], Z_STORES * (q + 2))
                settle(sp)
                for c in range(PCHUNKS):
                    src = bass.AP(z_dram.tensor, z_dram[h, c * IROWS, c * IROWS + 1, 0, 0:1].offset,
                                  [[(ZCOLS + 1) * HALF, IROWS], [HALF, NK], [1, HALF]])
                    sp.dma_start(pairs[:, c, h * HALF:(h + 1) * HALF], src).then_inc(pairs_loaded[h], 16)

            def store_y(q, h):
                sp.wait_ge(mlp_read, MLP_USES * (2 * q + h + 1) + 1)
                settle(sp)
                dst = out[bass.ds(q * QCOLS + h * HALF, HALF), :].rearrange("(t s g) o -> o s t g", t=2, s=SBLK)
                sp.dma_start(dst, y.rearrange("o (s t g) -> o s t g", s=SBLK, t=2)).then_inc(y_stored, 16)

            sp.sem_inc(y_stored, 16)
            for h in range(2):
                sp.sem_inc(z_stored[h], Z_STORES)
            sp.dma_start(idx[:, 0, :], ids[0:P, :]).then_inc(idx_loaded[0], 16)
            sp.dma_start(ids_int, ids_rows).then_inc(ids_loaded, 16)
            for t in range(1, TILES):
                sp.dma_start(idx[:, t, :], ids[t * P:(t + 1) * P, :]).then_inc(idx_loaded[t], 16)
            for k, f in enumerate(ONE_HOT):
                if k == RAW_BUFS:
                    sp.dma_start(dense_t[:], dense_cols).then_inc(dense_loaded, 16)
                if k >= RAW_BUFS:
                    sp.wait_ge(lo_made, k - RAW_BUFS + 1)
                sp.dma_start(raw[0:CROWS, k % RAW_BUFS, :], table_rows(f)).then_inc(raw_loaded[k % RAW_BUFS], 16)
            for dst, src in (
                (w1_sb[0:PCHUNK, 0:PCHUNKS, :], w1[0:PCHUNK * PCHUNKS, :].rearrange("(c p) n -> p c n", p=PCHUNK)),
                (w1_sb[:, PCHUNKS, :], w1[PCHUNK * PCHUNKS:PCHUNK * PCHUNKS + DIM, :]),
                (w2_sb[:], w2.rearrange("(c p) n -> p c n", p=P)),
                (w3_sb[:], w3),
                (b1_sb[:], b1),
                (b2_sb[:], b2),
            ):
                sp.dma_start(dst, src).then_inc(weights_loaded, 16)

            regroup(0, 1)
            with sp.Fori(0, QUARTERS - 1) as q:
                regroup(q, TILES - 1)
                store_y(q, 0)
                regroup(q + 1, 1)
                store_y(q, 1)
            regroup(QUARTERS - 1, TILES - 1)
            store_y(QUARTERS - 1, 0)
            store_y(QUARTERS - 1, 1)
            sp.wait_ge(y_stored, 16 * (2 * QUARTERS + 1))

        @block.gpsimd
        def _(pool):
            pool.memset(ident[:], 0.0).then_inc(cleared, 1)
            pool.memset(pick[:], 0.0).then_inc(cleared, 1)
            pool.iota(row_no_i[:], [[1, CHUNKS]], base=0, channel_multiplier=CHUNKS).then_inc(consts_made, 1)
            pool.wait_ge(cleared, 2)
            pool.affine_select(out=ident[:], in_=ident[:], compare_op=ALU.not_equal, fill=1.0, base=0,
                               pattern=[[-1, P]], channel_multiplier=1).then_inc(consts_made, 1)
            pool.affine_select(out=pick[:], in_=pick[:], compare_op=ALU.not_equal, fill=1.0, base=0,
                               pattern=[[-1, NO], [0, CROWS]], channel_multiplier=1).then_inc(consts_made, 1)

            def gather(t):
                for s, f in enumerate(GATHERED):
                    pool.indirect_dma_start(
                        rows[:, t, s, :], None, tables[f],
                        bass.IndirectOffsetOnAxis(ap=idx[:, t, f:f + 1], axis=0)).then_inc(gathered[t], 16)

            for t in range(TILES):
                pool.wait_ge(idx_loaded[t], 16)
                gather(t)
            with pool.Fori(1, QUARTERS) as q:
                for t in range(TILES):
                    pool.wait_ge(ring_filled, rows_read(q - 1, t))
                    pool.wait_ge(idx_loaded[t], 16 * (q + 1))
                    settle(pool)
                    gather(t)

        @block.tensor
        def _(pe):
            def spread(q, k):
                pe.wait_ge(one_hot_made, CHUNKS * (q * NO + k))
                settle(pe)
                pe.matmul(spread_ids[0:CROWS, :], pick[:, k, :], ids16[:, bass.ds(q * QCOLS, QCOLS)],
                          start=True, stop=True).then_inc(ids_spread, 1)

            def look_up(q, k, c):
                if c == CHUNKS - 2 and k + 1 < NO:
                    spread(q, k + 1)
                pe.wait_ge(one_hot_made, CHUNKS * (q * NO + k) + c + 1)
                if c == 0:
                    pe.wait_ge(table_read, q * NO + k)
                hot = one_hot[:, (k * CHUNKS + c) % OH_BUFS, :]
                pe.matmul(table_out[:], tab_hi[0:CROWS, k, c, :], hot, start=(c == 0), stop=False)
                pe.matmul(table_out[:], tab_lo[0:CROWS, k, c, :], hot, start=False,
                          stop=(c == CHUNKS - 1)).then_inc(one_hot_used, 1)

            def ring_free(q, t, u):
                if isinstance(q, int) and q * TILES + t == 0 and u < 2:
                    return
                by_act, by_dve = reads(q * TILES + t, u - 2) if u >= 2 else reads(q * TILES + t - 1, UNITS + u - 2)
                v = (u - 2) % UNITS
                if v != DVE_UNIT:
                    pe.wait_ge(ring_read_act, by_act)
                if v == DVE_UNIT or v >= len(T_UNITS):
                    pe.wait_ge(ring_read_dve, by_dve)

            def tile(q, t, chunks=(), between=None):
                if chunks and chunks[0] == 0:
                    spread(q + 1, 0)
                pe.wait_ge(gathered[t], 16 * NG * (q + 1))
                for u, (first, n) in enumerate(T_UNITS):
                    r = (UNITS * t + u) % 2
                    ring_free(q, t, u)
                    for i in range(n):
                        mm = pe.transpose(ring[r][:, i // 4, (i % 4) * P:(i % 4 + 1) * P],
                                          rows[:, t, first + i, :], ident[:])
                    mm.then_inc(ring_filled, 1)
                done = 0

                def look_ups(due):
                    nonlocal done
                    while chunks and done < due:
                        look_up(q + 1, *divmod(chunks[done], CHUNKS))
                        done += 1

                look_ups(chunks_due(len(chunks), 0))
                if between:
                    between()
                for gu in range(G_UNITS):
                    u = len(T_UNITS) + gu
                    r = (UNITS * t + u) % 2
                    if gu == 0:
                        pe.wait_ge(placed, q * TILES + t + 1)
                        by_act, by_dve = reads(q * TILES + t, len(T_UNITS) - 1)
                        pe.wait_ge(ring_read_act, by_act)
                        pe.wait_ge(ring_read_dve, by_dve)
                    ring_free(q, t, u)
                    for i in range(G_PER_UNIT):
                        g = gu * G_PER_UNIT + i
                        left = ct[:, t % 2, g].rearrange("p s f -> p (s f)")
                        right = ct[:, t % 2, g, :, 0:NF]
                        n = SBLK * NF
                        mm = pe.matmul(ring[r][:, i // 4, (i % 4) * n:(i % 4 + 1) * n], left, right,
                                       start=True, stop=True)
                        if i == G_PER_UNIT - 1:
                            mm.then_inc(ring_filled, 1)
                        look_ups(chunks_due(len(chunks), g + 1))

            def mlp_layers(q, h):
                used = MLP_USES * (2 * q + h)
                n1, n2 = HID1 // P, HID2 // P

                def bank(j):
                    pe.wait_ge(mlp_read, used + j if h + j else MLP_USES * 2 * q + 1)
                    return mlp[(h * MLP_USES + j) % 2]

                pe.wait_ge(pairs_loaded[h], 16 * PCHUNKS * (q + 1))
                here = slice(h * HALF, (h + 1) * HALF)
                dense_half = dense_t[:, bass.ds(q * QCOLS + h * HALF, HALF)].rearrange(
                    "p (t s g) -> p s t g", t=2, s=SBLK)
                for m in range(n1):
                    acc = bank(m)
                    cols = slice(m * P, (m + 1) * P)
                    for c in range(PCHUNKS):
                        pe.matmul(acc[:, 0:HALF], w1_sb[0:PCHUNK, c, cols], pairs[:, c, here],
                                  start=(c == 0), stop=False)
                    pe.matmul(acc[:, 0:HALF], w1_sb[:, PCHUNKS, cols], dense_half,
                              start=False, stop=True).then_inc(mlp_filled, 1)
                for m in range(n2):
                    acc = bank(n1 + m)
                    for c in range(n1):
                        if m == 0:
                            pe.wait_ge(mlp_read, used + c + 2)
                        mm = pe.matmul(acc[:, 0:HALF], w2_sb[:, c, m * P:(m + 1) * P], h1[:, c, :],
                                       start=(c == 0), stop=(c == n1 - 1))
                    mm.then_inc(mlp_filled, 1)
                acc = bank(n1 + n2)
                for c in range(n2):
                    pe.wait_ge(mlp_read, used + n1 + c + 2)
                    mm = pe.matmul(acc[0:1, 0:HALF], w3_sb[:, c:c + 1], h2[:, c, :],
                                   start=(c == 0), stop=(c == n2 - 1))
                mm.then_inc(mlp_filled, 1)

            pe.sem_inc(mlp_filled, MLP_USES + 1)
            pe.wait_ge(consts_made, 3)
            pe.wait_ge(ids_converted, 1)
            spread(0, 0)
            for k in range(NO):
                pe.wait_ge(lo_made, k + 1)
                for c in range(CHUNKS):
                    look_up(0, k, c)
            pe.wait_ge(padding_made, 2)
            tile(0, 0)
            pe.wait_ge(weights_loaded, 16 * 6)
            tile(0, 1)
            with pe.Fori(0, QUARTERS - 1) as q:
                tile(q, 2, chunks_in(2))
                tile(q, 3, chunks_in(3))
                tile(q + 1, 0, between=lambda: mlp_layers(q, 0))
                tile(q + 1, 1, between=lambda: mlp_layers(q, 1))
            tile(QUARTERS - 1, 2)
            tile(QUARTERS - 1, 3)
            mlp_layers(QUARTERS - 1, 0)
            mlp_layers(QUARTERS - 1, 1)

        @block.scalar
        def _(act):
            def read_table(q, k):
                act.wait_ge(one_hot_used, CHUNKS * (q * NO + k + 1))
                settle(act)
                act.copy(looked_up[:, q % 2, k, :], table_out[:]).then_inc(table_read, 1)

            def tile(q, t, chunks=(), between=None):
                slot = ct[:, t % 2].rearrange("p g s f -> p f s g")
                last = [(k, chunks.index(k * CHUNKS + CHUNKS - 1)) for k in range(NO)
                        if k * CHUNKS + CHUNKS - 1 in chunks]
                for u in range(len(T_UNITS)):
                    if u != DVE_UNIT:
                        act.wait_ge(ring_filled, UNITS * (q * TILES + t) + u + 1)
                        act.copy(*transposed_unit(t, u)).then_inc(ring_read_act, 1)
                act.wait_ge(table_read, NO * (q + 1))
                settle(act)
                for k in range(NO):
                    act.copy(slot[:, k], looked_up[:, q % 2, k, t * P:(t + 1) * P].rearrange(
                        "p (s g) -> p s g", s=SBLK))
                act.copy(slot[:, NF - 1], dense_t[:, bass.ds((q * TILES + t) * P, P)].rearrange(
                    "p (s g) -> p s g", s=SBLK)).then_inc(placed, 1)
                if not isinstance(q, int) or q < QUARTERS - 1:
                    act.dma_start(idx[:, t, :], ids[bass.ds(((q + 1) % QUARTERS * TILES + t) * P, P), :]).then_inc(
                        idx_loaded[t], 16)
                if between:
                    between()
                for gu in range(G_UNITS):
                    u = len(T_UNITS) + gu
                    for k, n in last:
                        if issued_before(n, chunks) // G_PER_UNIT == gu:
                            read_table(q + 1, k)
                    act.wait_ge(ring_filled, UNITS * (q * TILES + t) + u + 1)
                    if gu == 0 and t % 2 == 0:
                        act.wait_ge(z_stored[t // 2], Z_STORES * (q + 1))
                    act.copy(z_view(t, gu, 0), gram_view((UNITS * t + u) % 2, 0))
                    act.copy(z_view(t, gu, 1), gram_view((UNITS * t + u) % 2, 1)).then_inc(ring_read_act, 1)
                for k, n in last:
                    if issued_before(n, chunks) == GROUPS:
                        read_table(q + 1, k)

            def mlp_layers(q, h):
                used = MLP_USES * (2 * q + h)
                n1, n2 = HID1 // P, HID2 // P
                for j in range(n1 + n2):
                    act.wait_ge(mlp_filled, used + MLP_USES + j + 2)
                    dst, bias = (h1[:, j, :], b1_sb[:, j:j + 1]) if j < n1 else (h2[:, j - n1, :],
                                                                                 b2_sb[:, j - n1:j - n1 + 1])
                    act.activation(dst, mlp[(h * MLP_USES + j) % 2][:, 0:HALF], ACT.Relu, bias=bias).then_inc(
                        mlp_read, 1)
                act.wait_ge(mlp_filled, used + 2 * MLP_USES + 1)
                act.wait_ge(y_stored, 16 * (2 * q + h + 1))
                act.copy(y, mlp[(h * MLP_USES + n1 + n2) % 2][0:1, 0:HALF]).then_inc(mlp_read, 1)

            act.sem_inc(mlp_read, 1)
            act.wait_ge(ids_loaded, 16)
            act.copy(ids16, ids_int).then_inc(ids_converted, 1)
            for k in range(NO):
                act.wait_ge(raw_loaded[k % RAW_BUFS], 16 * (k // RAW_BUFS + 1))
                act.copy(tab_hi[0:CROWS, k].rearrange("p c d -> p (c d)"), raw[0:CROWS, k % RAW_BUFS, :]).then_inc(
                    hi_made, 1)
                if k >= 1:
                    read_table(0, k - 1)
            act.wait_ge(lo_made, NO)
            act.wait_ge(zero_made, 1)
            act.copy(z[:].rearrange("p h f g -> p (h f g)"), zero[:].broadcast_to([P, 2 * NF * HALF_G])).then_inc(
                padding_made, 1)
            read_table(0, NO - 1)
            act.wait_ge(padding_made, 2)
            act.wait_ge(dense_loaded, 16)
            tile(0, 0)
            act.wait_ge(weights_loaded, 16 * 6)
            tile(0, 1)
            with act.Fori(0, QUARTERS - 1) as q:
                tile(q, 2, chunks_in(2))
                tile(q, 3, chunks_in(3))
                tile(q + 1, 0, between=lambda: mlp_layers(q, 0))
                tile(q + 1, 1, between=lambda: mlp_layers(q, 1))
            tile(QUARTERS - 1, 2)
            tile(QUARTERS - 1, 3)
            mlp_layers(QUARTERS - 1, 0)
            mlp_layers(QUARTERS - 1, 1)
            for t in range(2):
                act.wait_ge(idx_loaded[t], 16 * (QUARTERS + 1))

        @block.vector
        def _(dve):
            def compare(q, k, c):
                if c == 0:
                    dve.wait_ge(ids_spread, q * NO + k + 1)
                if not (isinstance(q, int) and q * NO + k == 0 and c < OH_BUFS):
                    dve.wait_ge(one_hot_used, CHUNKS * (q * NO + k) + c - OH_BUFS + 1)
                dve.tensor_scalar(one_hot[:, (k * CHUNKS + c) % OH_BUFS, :], spread_ids[0:CROWS, :], row_no[0:CROWS, c:c + 1],
                                  None, ALU.is_equal).then_inc(one_hot_made, 1)

            def read_unit(q, t, gu):
                u = len(T_UNITS) + gu
                dve.wait_ge(ring_filled, UNITS * (q * TILES + t) + u + 1)
                if gu == 0 and t % 2 == 0:
                    dve.wait_ge(z_stored[t // 2], Z_STORES * (q + 1))
                dve.tensor_copy(z_view(t, gu, 2), gram_view((UNITS * t + u) % 2, 2))
                dve.tensor_copy(z_view(t, gu, 3), gram_view((UNITS * t + u) % 2, 3)).then_inc(ring_read_dve, 1)

            def read_transposed(q, t):
                dve.wait_ge(ring_filled, UNITS * (q * TILES + t) + DVE_UNIT + 1)
                dve.tensor_copy(*transposed_unit(t, DVE_UNIT)).then_inc(ring_read_dve, 1)

            def tile(q, t, chunks=()):
                after = [chunks_due(len(chunks), (gu + 1) * G_PER_UNIT - 1) + 2 for gu in range(G_UNITS)]
                for n, chunk in enumerate(chunks):
                    compare(q + 1, *divmod(chunk, CHUNKS))
                    if n == DVE_AHEAD:
                        read_transposed(q, t)
                    if n in after:
                        read_unit(q, t, after.index(n))
                if not chunks:
                    read_transposed(q, t)
                for gu in range(G_UNITS):
                    if not chunks or after[gu] >= len(chunks):
                        read_unit(q, t, gu)

            dve.wait_ge(consts_made, 3)
            dve.tensor_copy(row_no[:], row_no_i[:]).then_inc(row_no_made, 1)
            dve.memset(zero[:], 0.0).then_inc(zero_made, 1)
            dve.wait_ge(row_no_made, 1)
            for k in range(NO):
                dve.wait_ge(hi_made, k + 1)
                dve.tensor_tensor(tab_lo[0:CROWS, k].rearrange("p c d -> p (c d)"), raw[0:CROWS, k % RAW_BUFS, :],
                                  tab_hi[0:CROWS, k].rearrange("p c d -> p (c d)").bitcast(F32),
                                  ALU.subtract).then_inc(lo_made, 1)
                for c in range(CHUNKS):
                    compare(0, k, c)
                if k == 0:
                    dve.wait_ge(ids_converted, 1)
                    dve.memset(ct[:, :, :, :, NF:FPAD], 0.0).then_inc(padding_made, 1)
            dve.wait_ge(padding_made, 2)
            tile(0, 0)
            tile(0, 1)
            with dve.Fori(0, QUARTERS - 1) as q:
                tile(q, 2, chunks_in(2))
                tile(q, 3, chunks_in(3))
                tile(q + 1, 0)
                tile(q + 1, 1)
            tile(QUARTERS - 1, 2)
            tile(QUARTERS - 1, 3)


def kernel(**inputs):
    import concourse.bacc as bacc
    from concourse.bass_utils import run_bass_kernel_spmd

    nc = bacc.Bacc("TRN2", target_bir_lowering=False, num_devices=1)
    ids = np.asarray(inputs["ids"])
    arrays = {name: np.asarray(inputs[name]) for name in
              ["W_top2"] + [f"tbl_{f}" for f in range(TABLES)]}
    arrays["ids"] = ids
    arrays["ids_rows"] = ids.T[ONE_HOT]
    arrays["dense_cols"] = np.asarray(inputs["r_dense_x"]).T
    arrays["W_top1"] = np.asarray(inputs["W_top1"])[pair_rows()]
    for name in ("b_top1", "b_top2", "W_top3"):
        arrays[name] = np.asarray(inputs[name]).reshape(-1, P).T
    feed, aps = {}, {}
    for name, a in arrays.items():
        a = np.ascontiguousarray(a)
        feed[f"in_{name}"] = a
        aps[name] = nc.dram_tensor(f"in_{name}", a.shape, mybir.dt.from_np(a.dtype), kind="ExternalInput").ap()
    out = nc.dram_tensor("out", (BATCH, 1), F32, kind="ExternalOutput").ap()
    dlrm(nc, aps["dense_cols"], aps["ids"], aps["ids_rows"], [aps[f"tbl_{f}"] for f in range(TABLES)],
         aps["W_top1"], aps["b_top1"], aps["W_top2"], aps["b_top2"], aps["W_top3"], out)
    return run_bass_kernel_spmd(nc, [feed], core_ids=[0]).results[0]["out"]
```

```python
from contextlib import ExitStack

import numpy as np

import concourse.bass as bass
from concourse import mybir

F32 = mybir.dt.float32
F32R = mybir.dt.float32r
F16 = mybir.dt.float16
I32 = mybir.dt.int32
ALU = mybir.AluOpType
ACT = mybir.ActivationFunctionType

P = 128
BATCH = 2048
DIM = 128
TABLES = 26
NF = TABLES + 1
QUARTERS = 4
TILES = 4
QCOLS = TILES * P
HID1, HID2 = 512, 256

ONE_HOT = [0, 1, 4, 8, 9, 13]
ONE_HOT_ROWS = 1000
GATHERED = [f for f in range(TABLES) if f not in ONE_HOT]
FEATURES = ONE_HOT + GATHERED + [TABLES]
NO = len(ONE_HOT)
NG = len(GATHERED)
CHUNKS = 8
CROWS = ONE_HOT_ROWS // CHUNKS
OH_BUFS = 3 if NO % 3 == 0 else 4
DVE_AHEAD = OH_BUFS - 1
RAW_BUFS = 3

SBLK = 4
GROUPS = P // SBLK
T_UNITS = [(a, min(8, NG - a)) for a in range(0, NG, 8)]
G_UNITS = 4
G_PER_UNIT = GROUPS // G_UNITS
UNITS = len(T_UNITS) + G_UNITS
HALF_G = 2 * GROUPS
NK = (NF - 1) // 2
ZCOLS = NF + NK
IROWS = 9
PCHUNK = IROWS * NK
PCHUNKS = NF // IROWS
HALF = QCOLS // 2
MLP_USES = HID1 // P + HID2 // P + 1
Z_STORES = 16 * 2 * SBLK
T_AFTER = 3
ACT_CHUNKS = [3, 7]
LEAD = 4
DVE_UNIT = 1


def chunks_in(t):
    return list(range(NO * CHUNKS * (t - 2) // 2, NO * CHUNKS * (t - 1) // 2))


def chunks_due(n, products):
    return LEAD + products * (n - LEAD) // GROUPS


def reads(tile, u):
    act = [v for v in range(u + 1) if v != DVE_UNIT]
    dve = [v for v in range(u + 1) if v == DVE_UNIT or v >= len(T_UNITS)]
    return (UNITS - 1) * tile + len(act), (G_UNITS + 1) * tile + len(dve)


FPAD = 32


def pair_rows():
    rows = []
    for i in range(NF):
        for k in range(1, NK + 1):
            a, b = sorted((FEATURES[i], FEATURES[(i + k) % NF]))
            rows.append(a * (NF - 1) - a * (a - 1) // 2 + b - a - 1)
    return np.array(rows + list(range(len(rows), len(rows) + DIM)))


def dlrm(nc, dense_cols, ids, ids_rows, tables, w1, b1, w2, b2, w3, out):
    with ExitStack() as ctx:
        def sb(name, shape, dt=F32):
            return ctx.enter_context(nc.sbuf_tensor(name, shape, dt))

        def ps(name, shape):
            return ctx.enter_context(nc.psum_tensor(name, shape, F32))

        def sem(name):
            return ctx.enter_context(nc.semaphore(name))

        tab_hi = sb("tab_hi", [P, NO, CHUNKS, DIM], F32R)
        tab_lo = sb("tab_lo", [P, NO, CHUNKS, DIM], F32R)
        looked_up = sb("looked_up", [P, 2, NO, QCOLS])
        rows = sb("rows", [P, TILES, NG, DIM])
        ct = sb("ct", [P, 2, GROUPS, SBLK, FPAD])
        z = sb("z", [P, 2, NF, HALF_G])
        pairs = sb("pairs", [PCHUNK, PCHUNKS, QCOLS])
        dense_t = sb("dense_t", [P, BATCH])
        h1 = sb("h1", [P, HID1 // P, HALF])
        h2 = sb("h2", [P, HID2 // P, HALF])
        w1_sb = sb("w1_sb", [P, PCHUNKS + 1, HID1])
        w2_sb = sb("w2_sb", [P, HID1 // P, HID2])
        w3_sb = sb("w3_sb", [P, HID2 // P])
        b1_sb = sb("b1_sb", [P, HID1 // P])
        b2_sb = sb("b2_sb", [P, HID2 // P])
        one_hot = sb("one_hot", [CROWS, OH_BUFS, QCOLS], F32R)
        small = sb("small", [33, BATCH // 2])
        ids16 = small[0:NO, :].bitcast(F16)
        y = small[32:33, 0:HALF]
        one = sb("one", [P, 1])
        minus_row = sb("minus_row", [P, CHUNKS])
        distance = sb("distance", [CROWS, QCOLS])
        pick = sb("pick", [NO, NO, CROWS], F16)
        row_no_i = sb("row_no_i", [P, CHUNKS], I32)
        row_no = sb("row_no", [P, CHUNKS])
        ident = sb("ident", [P, P])
        idx = sb("idx", [P, TILES, TABLES], I32)
        raw = z[:].rearrange("p h f g -> p (h f g)")[:, 0:RAW_BUFS * CHUNKS * DIM].rearrange(
            "p (r n) -> p r n", r=RAW_BUFS)
        ids_int = ct[0:NO, 0].rearrange("p g s f -> p (g s f)")[:, 0:BATCH].bitcast(I32)

        ring = [ps(f"ring{r}", [P, 2, 512]) for r in range(2)]
        spread_ids = ps("spread_ids", [P, 512])
        table_out = ps("table_out", [P, 512])
        mlp = [ps(f"mlp{r}", [P, 512]) for r in range(2)]
        spread_bank = [spread_ids, mlp[1]]
        table_bank = [table_out, mlp[0]]

        z_dram = nc.dram_tensor("z_dram", [2, NF, ZCOLS, SBLK, HALF_G], F32, kind="Internal").ap()

        idx_loaded = [sem(f"idx_loaded{t}") for t in range(TILES)]
        dense_loaded = sem("dense_loaded")
        gathered = [sem(f"gathered{t}") for t in range(TILES)]
        ids_loaded = sem("ids_loaded")
        ids_converted = sem("ids_converted")
        raw_loaded = [sem(f"raw_loaded{r}") for r in range(RAW_BUFS)]
        hi_made = sem("hi_made")
        lo_made = sem("lo_made")
        cleared = sem("cleared")
        consts_made = sem("consts_made")
        row_no_made = sem("row_no_made")
        padding_made = sem("padding_made")
        weights_loaded = sem("weights_loaded")
        ids_spread = sem("ids_spread")
        ids_spread_act = sem("ids_spread_act")
        one_hot_made = sem("one_hot_made")
        one_hot_made_act = sem("one_hot_made_act")
        distance_made = sem("distance_made")
        minus_row_made = sem("minus_row_made")
        one_hot_used = sem("one_hot_used")
        table_read = sem("table_read")
        placed = sem("placed")
        ring_filled = sem("ring_filled")
        ring_read_act = sem("ring_read_act")
        ring_read_dve = sem("ring_read_dve")
        z_stored = [sem(f"z_stored{h}") for h in range(2)]
        pairs_loaded = [sem(f"pairs_loaded{h}") for h in range(2)]
        mlp_filled = sem("mlp_filled")
        mlp_read = sem("mlp_read")
        y_stored = sem("y_stored")
        settled = sem("settled")

        block = ctx.enter_context(nc.Block())

        def settle(eng):
            eng.sem_inc(settled, 1)

        def first_quarter(q):
            return isinstance(q, int) and q == 0

        def made(q, k, n):
            by_act = (k if first_quarter(q) else NO) * len(ACT_CHUNKS)
            if first_quarter(q):
                by_act += len([c for c in ACT_CHUNKS if c < n])
            return CHUNKS * (q * NO + k) + n - by_act

        def rows_read(q, t):
            return UNITS * (q * TILES + t) + len(T_UNITS)

        def table_rows(f):
            return tables[f].rearrange("(p c) d -> p (c d)", c=CHUNKS)

        def issued_before(n, chunks):
            return min(p for p in range(GROUPS + 1) if chunks_due(len(chunks), p) > n)

        def transposed_unit(t, u):
            first, n = T_UNITS[u]
            dst = ct[:, t % 2].rearrange("p g s f -> p f s g")[:, NO + first:NO + first + n]
            src = ring[(UNITS * t + u) % 2][:].rearrange("p b n -> p (b n)")[:, 0:n * P]
            return dst, src.rearrange("p (k s g) -> p k s g", k=n, s=SBLK)

        def gram_view(r, s):
            return ring[r][32 * s:32 * s + NF, :, 0:4 * SBLK * NF].rearrange(
                "p b (g s f) -> p b g s f", g=4, s=SBLK)[:, :, :, s, :]

        def z_view(t, gu, s):
            at = (t % 2) * GROUPS + gu * G_PER_UNIT
            return z[32 * s:32 * s + NF, t // 2, :, at:at + G_PER_UNIT].rearrange(
                "p f (b g) -> p b g f", b=2)

        @block.sync
        def _(sp):
            def regroup(q, t):
                h = t // 2
                by_act, by_dve = reads(q * TILES + t, UNITS - 1)
                sp.wait_ge(mlp_filled, MLP_USES * (2 * q + h) + 1)
                settle(sp)
                for s in range(SBLK):
                    if s == 0:
                        sp.wait_ge(ring_read_act, by_act)
                        settle(sp)
                    if s == SBLK // 2:
                        sp.wait_ge(ring_read_dve, by_dve)
                        settle(sp)
                    block = z[32 * s:32 * s + NF, h, :, :]
                    dst = z_dram[h, :, :, s, :]
                    sp.dma_start(dst[:, 0:NF, :], block).then_inc(z_stored[h], 16)
                    sp.dma_start(dst[:, NF:ZCOLS, :], block[:, 0:NK, :]).then_inc(z_stored[h], 16)
                sp.wait_ge(z_stored[h], Z_STORES * (q + 2))
                settle(sp)
                for c in range(PCHUNKS):
                    src = bass.AP(z_dram.tensor, z_dram[h, c * IROWS, c * IROWS + 1, 0, 0:1].offset,
                                  [[(ZCOLS + 1) * HALF, IROWS], [HALF, NK], [1, HALF]])
                    sp.dma_start(pairs[:, c, h * HALF:(h + 1) * HALF], src).then_inc(pairs_loaded[h], 16)

            def store_y(q, h):
                sp.wait_ge(mlp_read, MLP_USES * (2 * q + h + 1) + 1)
                settle(sp)
                dst = out[bass.ds(q * QCOLS + h * HALF, HALF), :].rearrange("(t s g) o -> o s t g", t=2, s=SBLK)
                sp.dma_start(dst, y.rearrange("o (s t g) -> o s t g", s=SBLK, t=2)).then_inc(y_stored, 16)

            sp.sem_inc(y_stored, 16)
            for h in range(2):
                sp.sem_inc(z_stored[h], Z_STORES)
            sp.dma_start(idx[:, 0, :], ids[0:P, :]).then_inc(idx_loaded[0], 16)
            sp.dma_start(ids_int, ids_rows).then_inc(ids_loaded, 16)
            for k, f in enumerate(ONE_HOT):
                if k == RAW_BUFS:
                    sp.dma_start(dense_t[:], dense_cols).then_inc(dense_loaded, 16)
                if k >= RAW_BUFS:
                    sp.wait_ge(lo_made, k - RAW_BUFS + 1)
                sp.dma_start(raw[0:CROWS, k % RAW_BUFS, :], table_rows(f)).then_inc(raw_loaded[k % RAW_BUFS], 16)
                if k == 0:
                    for t in range(1, TILES):
                        sp.dma_start(idx[:, t, :], ids[t * P:(t + 1) * P, :]).then_inc(idx_loaded[t], 16)
            for dst, src in (
                (w1_sb[0:PCHUNK, 0:PCHUNKS, :], w1[0:PCHUNK * PCHUNKS, :].rearrange("(c p) n -> p c n", p=PCHUNK)),
                (w1_sb[:, PCHUNKS, :], w1[PCHUNK * PCHUNKS:PCHUNK * PCHUNKS + DIM, :]),
                (w2_sb[:], w2.rearrange("(c p) n -> p c n", p=P)),
                (w3_sb[:], w3),
                (b1_sb[:], b1),
                (b2_sb[:], b2),
            ):
                sp.dma_start(dst, src).then_inc(weights_loaded, 16)

            regroup(0, 1)
            with sp.Fori(0, QUARTERS - 1) as q:
                regroup(q, TILES - 1)
                store_y(q, 0)
                regroup(q + 1, 1)
                store_y(q, 1)
            regroup(QUARTERS - 1, TILES - 1)
            store_y(QUARTERS - 1, 0)
            store_y(QUARTERS - 1, 1)
            sp.wait_ge(y_stored, 16 * (2 * QUARTERS + 1))

        @block.gpsimd
        def _(pool):
            pool.memset(ident[:], 0.0).then_inc(cleared, 1)
            pool.memset(pick[:], 0.0).then_inc(cleared, 1)
            pool.iota(row_no_i[:], [[1, CHUNKS]], base=0, channel_multiplier=CHUNKS).then_inc(consts_made, 1)
            pool.wait_ge(cleared, 2)
            pool.affine_select(out=ident[:], in_=ident[:], compare_op=ALU.not_equal, fill=1.0, base=0,
                               pattern=[[-1, P]], channel_multiplier=1).then_inc(consts_made, 1)
            pool.affine_select(out=pick[:], in_=pick[:], compare_op=ALU.not_equal, fill=1.0, base=0,
                               pattern=[[-1, NO], [0, CROWS]], channel_multiplier=1).then_inc(consts_made, 1)

            def gather(t):
                for s, f in enumerate(GATHERED):
                    pool.indirect_dma_start(
                        rows[:, t, s, :], None, tables[f],
                        bass.IndirectOffsetOnAxis(ap=idx[:, t, f:f + 1], axis=0)).then_inc(gathered[t], 16)

            for t in range(TILES):
                pool.wait_ge(idx_loaded[t], 16)
                gather(t)
            with pool.Fori(1, QUARTERS) as q:
                for t in range(TILES):
                    pool.wait_ge(ring_filled, rows_read(q - 1, t))
                    pool.wait_ge(idx_loaded[t], 16 * (q + 1))
                    settle(pool)
                    gather(t)

        @block.tensor
        def _(pe):
            def mlp_read_before(q):
                pe.wait_ge(mlp_read, MLP_USES * 2 * (q - 1) + 1)
                settle(pe)

            def spread(q, k):
                if first_quarter(q):
                    if k:
                        pe.wait_ge(one_hot_made, made(q, k, 0))
                    pe.matmul(spread_ids[0:CROWS, :], pick[:, k, :], ids16[:, 0:QCOLS],
                              start=True, stop=True).then_inc(ids_spread, 1)
                    if k:
                        pe.wait_ge(one_hot_made_act, len(ACT_CHUNKS) * k)
                    pe.matmul(mlp[1][0:CROWS, :], pick[:, k, :], ids16[:, 0:QCOLS],
                              start=True, stop=True).then_inc(ids_spread_act, 1)
                else:
                    pe.wait_ge(one_hot_made, made(q, max(k - 1, 0), 0))
                    settle(pe)
                    if k == 1:
                        mlp_read_before(q)
                    pe.matmul(spread_bank[k % 2][0:CROWS, :], pick[:, k, :], ids16[:, bass.ds(q * QCOLS, QCOLS)],
                              start=True, stop=True).then_inc(ids_spread, 1)

            def look_up(q, k, c):
                if c == (CHUNKS - 2 if first_quarter(q) else 1) and k + 1 < NO:
                    spread(q, k + 1)
                if c == 0 and k == 1 and not first_quarter(q):
                    mlp_read_before(q)
                if first_quarter(q) and c in ACT_CHUNKS:
                    pe.wait_ge(one_hot_made_act, len(ACT_CHUNKS) * k + ACT_CHUNKS.index(c) + 1)
                else:
                    pe.wait_ge(one_hot_made, made(q, k, c + 1))
                if c == 0 and not (first_quarter(q) and k < 2):
                    pe.wait_ge(table_read, q * NO + max(k - 1, 0))
                hot = one_hot[:, (k * CHUNKS + c) % OH_BUFS, :]
                pe.matmul(table_bank[k % 2][:], tab_hi[0:CROWS, k, c, :], hot, start=(c == 0), stop=False)
                pe.matmul(table_bank[k % 2][:], tab_lo[0:CROWS, k, c, :], hot, start=False,
                          stop=(c == CHUNKS - 1)).then_inc(one_hot_used, 1)

            def ring_free(q, t, u):
                if isinstance(q, int) and q * TILES + t == 0 and u < 2:
                    return
                by_act, by_dve = reads(q * TILES + t, u - 2) if u >= 2 else reads(q * TILES + t - 1, UNITS + u - 2)
                v = (u - 2) % UNITS
                if v != DVE_UNIT:
                    pe.wait_ge(ring_read_act, by_act)
                if v == DVE_UNIT or v >= len(T_UNITS):
                    pe.wait_ge(ring_read_dve, by_dve)

            def tile(q, t, chunks=(), between=None):
                if chunks and chunks[0] == 0:
                    spread(q + 1, 0)
                transposes(q, t)
                products(q, t, chunks, between)

            def transposes(q, t):
                pe.wait_ge(gathered[t], 16 * NG * (q + 1))
                for u, (first, n) in enumerate(T_UNITS):
                    r = (UNITS * t + u) % 2
                    ring_free(q, t, u)
                    for i in range(n):
                        mm = pe.transpose(ring[r][:, i // 4, (i % 4) * P:(i % 4 + 1) * P],
                                          rows[:, t, first + i, :], ident[:])
                    mm.then_inc(ring_filled, 1)

            def products(q, t, chunks=(), between=None):
                done = 0

                def look_ups(due):
                    nonlocal done
                    while chunks and done < due:
                        look_up(q + 1, *divmod(chunks[done], CHUNKS))
                        done += 1

                look_ups(chunks_due(len(chunks), 0))
                if between:
                    between()
                for gu in range(G_UNITS):
                    u = len(T_UNITS) + gu
                    r = (UNITS * t + u) % 2
                    if gu == 0:
                        pe.wait_ge(placed, q * TILES + t + 1)
                        by_act, by_dve = reads(q * TILES + t, len(T_UNITS) - 1)
                        pe.wait_ge(ring_read_act, by_act)
                        pe.wait_ge(ring_read_dve, by_dve)
                    ring_free(q, t, u)
                    for i in range(G_PER_UNIT):
                        g = gu * G_PER_UNIT + i
                        left = ct[:, t % 2, g].rearrange("p s f -> p (s f)")
                        right = ct[:, t % 2, g, :, 0:NF]
                        n = SBLK * NF
                        mm = pe.matmul(ring[r][:, i // 4, (i % 4) * n:(i % 4 + 1) * n], left, right,
                                       start=True, stop=True)
                        if i == G_PER_UNIT - 1:
                            mm.then_inc(ring_filled, 1)
                        look_ups(chunks_due(len(chunks), g + 1))

            def mlp_layers(q, h):
                used = MLP_USES * (2 * q + h)
                n1, n2 = HID1 // P, HID2 // P

                def bank(j):
                    pe.wait_ge(mlp_read, used + j if h + j else MLP_USES * 2 * q + 1)
                    return mlp[(h * MLP_USES + j) % 2]

                pe.wait_ge(pairs_loaded[h], 16 * PCHUNKS * (q + 1))
                if h == 0 and not isinstance(q, int):
                    pe.wait_ge(table_read, NO * (q + 2))
                here = slice(h * HALF, (h + 1) * HALF)
                dense_half = dense_t[:, bass.ds(q * QCOLS + h * HALF, HALF)].rearrange(
                    "p (t s g) -> p s t g", t=2, s=SBLK)
                for m in range(n1):
                    acc = bank(m)
                    cols = slice(m * P, (m + 1) * P)
                    for c in range(PCHUNKS):
                        pe.matmul(acc[:, 0:HALF], w1_sb[0:PCHUNK, c, cols], pairs[:, c, here],
                                  start=(c == 0), stop=False)
                    pe.matmul(acc[:, 0:HALF], w1_sb[:, PCHUNKS, cols], dense_half,
                              start=False, stop=True).then_inc(mlp_filled, 1)
                for m in range(n2):
                    acc = bank(n1 + m)
                    for c in range(n1):
                        if m == 0:
                            pe.wait_ge(mlp_read, used + c + 2)
                        mm = pe.matmul(acc[:, 0:HALF], w2_sb[:, c, m * P:(m + 1) * P], h1[:, c, :],
                                       start=(c == 0), stop=(c == n1 - 1))
                    mm.then_inc(mlp_filled, 1)
                acc = bank(n1 + n2)
                for c in range(n2):
                    pe.wait_ge(mlp_read, used + n1 + c + 2)
                    mm = pe.matmul(acc[0:1, 0:HALF], w3_sb[:, c:c + 1], h2[:, c, :],
                                   start=(c == 0), stop=(c == n2 - 1))
                mm.then_inc(mlp_filled, 1)

            pe.sem_inc(mlp_filled, MLP_USES + 1)
            pe.wait_ge(consts_made, 3)
            pe.wait_ge(ids_converted, 1)
            spread(0, 0)
            for k in range(NO):
                pe.wait_ge(lo_made, k + 1)
                for c in range(CHUNKS):
                    look_up(0, k, c)
                if k == T_AFTER:
                    transposes(0, 0)
            pe.wait_ge(padding_made, 1)
            products(0, 0)
            pe.wait_ge(weights_loaded, 16 * 6)
            tile(0, 1)
            with pe.Fori(0, QUARTERS - 1) as q:
                tile(q, 2, chunks_in(2))
                tile(q, 3, chunks_in(3))
                tile(q + 1, 0, between=lambda: mlp_layers(q, 0))
                tile(q + 1, 1, between=lambda: mlp_layers(q, 1))
            tile(QUARTERS - 1, 2)
            tile(QUARTERS - 1, 3)
            mlp_layers(QUARTERS - 1, 0)
            mlp_layers(QUARTERS - 1, 1)

        @block.scalar
        def _(act):
            def read_table(q, k):
                act.wait_ge(one_hot_used, CHUNKS * (q * NO + k + 1))
                settle(act)
                act.copy(looked_up[:, q % 2, k, :], table_bank[k % 2][:]).then_inc(table_read, 1)

            def compare(k, c):
                n = k * len(ACT_CHUNKS) + ACT_CHUNKS.index(c)
                act.wait_ge(ids_spread_act, k + 1)
                if n:
                    act.wait_ge(one_hot_made_act, n)
                act.activation(distance[:], mlp[1][0:CROWS, :], ACT.Abs, bias=minus_row[0:CROWS, c:c + 1]).then_inc(
                    distance_made, 1)
                act.wait_ge(distance_made, n + 1)
                if k * CHUNKS + c >= OH_BUFS:
                    act.wait_ge(one_hot_used, CHUNKS * k + c - OH_BUFS + 1)
                act.activation(one_hot[:, (k * CHUNKS + c) % OH_BUFS, :], distance[:], ACT.Relu,
                               bias=one[0:CROWS, :], scale=-1.0).then_inc(one_hot_made_act, 1)

            def read_transposed(q, t):
                for u in range(len(T_UNITS)):
                    if u != DVE_UNIT:
                        act.wait_ge(ring_filled, UNITS * (q * TILES + t) + u + 1)
                        act.copy(*transposed_unit(t, u)).then_inc(ring_read_act, 1)

            def place_table(q, t, k):
                return act.copy(ct[:, t % 2].rearrange("p g s f -> p f s g")[:, k],
                                looked_up[:, q % 2, k, t * P:(t + 1) * P].rearrange("p (s g) -> p s g", s=SBLK))

            def place_dense(q, t):
                return act.copy(ct[:, t % 2].rearrange("p g s f -> p f s g")[:, NF - 1],
                                dense_t[:, bass.ds((q * TILES + t) * P, P)].rearrange("p (s g) -> p s g", s=SBLK))

            def place(q, t):
                act.wait_ge(table_read, NO * (q + 1))
                settle(act)
                for k in range(NO):
                    place_table(q, t, k)
                place_dense(q, t).then_inc(placed, 1)

            def tile(q, t, chunks=(), between=None):
                last = [(k, chunks.index(k * CHUNKS + CHUNKS - 1)) for k in range(NO)
                        if k * CHUNKS + CHUNKS - 1 in chunks]
                if not (isinstance(q, int) and q * TILES + t == 0):
                    read_transposed(q, t)
                if t == 0 and not isinstance(q, int):
                    place(q, 0)
                if not isinstance(q, int) or q < QUARTERS - 1:
                    act.dma_start(idx[:, t, :], ids[bass.ds(((q + 1) % QUARTERS * TILES + t) * P, P), :]).then_inc(
                        idx_loaded[t], 16)
                if between:
                    between()
                if t < TILES - 1:
                    place(q, t + 1)
                for gu in range(G_UNITS):
                    u = len(T_UNITS) + gu
                    for k, n in last:
                        if issued_before(n, chunks) // G_PER_UNIT == gu:
                            read_table(q + 1, k)
                    act.wait_ge(ring_filled, UNITS * (q * TILES + t) + u + 1)
                    if gu == 0 and t % 2 == 0:
                        act.wait_ge(z_stored[t // 2], Z_STORES * (q + 1))
                    act.copy(z_view(t, gu, 0), gram_view((UNITS * t + u) % 2, 0))
                    act.copy(z_view(t, gu, 1), gram_view((UNITS * t + u) % 2, 1)).then_inc(ring_read_act, 1)
                for k, n in last:
                    if issued_before(n, chunks) == GROUPS:
                        read_table(q + 1, k)

            def mlp_layers(q, h):
                used = MLP_USES * (2 * q + h)
                n1, n2 = HID1 // P, HID2 // P
                for j in range(n1 + n2):
                    act.wait_ge(mlp_filled, used + MLP_USES + j + 2)
                    dst, bias = (h1[:, j, :], b1_sb[:, j:j + 1]) if j < n1 else (h2[:, j - n1, :],
                                                                                 b2_sb[:, j - n1:j - n1 + 1])
                    act.activation(dst, mlp[(h * MLP_USES + j) % 2][:, 0:HALF], ACT.Relu, bias=bias).then_inc(
                        mlp_read, 1)
                act.wait_ge(mlp_filled, used + 2 * MLP_USES + 1)
                act.wait_ge(y_stored, 16 * (2 * q + h + 1))
                act.copy(y, mlp[(h * MLP_USES + n1 + n2) % 2][0:1, 0:HALF]).then_inc(mlp_read, 1)

            def split_high(k):
                act.wait_ge(raw_loaded[k % RAW_BUFS], 16 * (k // RAW_BUFS + 1))
                act.copy(tab_hi[0:CROWS, k].rearrange("p c d -> p (c d)"), raw[0:CROWS, k % RAW_BUFS, :]).then_inc(
                    hi_made, 1)

            act.sem_inc(mlp_read, 1)
            act.wait_ge(ids_loaded, 16)
            act.copy(ids16, ids_int).then_inc(ids_converted, 1)
            split_high(0)
            act.wait_ge(row_no_made, 2)
            act.activation(minus_row[:], row_no[:], ACT.Copy, scale=-1.0).then_inc(minus_row_made, 1)
            act.wait_ge(minus_row_made, 1)
            for k in range(NO):
                if k + 1 < NO:
                    split_high(k + 1)
                if k >= 1:
                    read_table(0, k - 1)
                compare(k, ACT_CHUNKS[0])
                compare(k, ACT_CHUNKS[1])
                if k == T_AFTER:
                    read_transposed(0, 0)
            act.wait_ge(dense_loaded, 16)
            act.wait_ge(table_read, NO - 1)
            for k in range(NO - 1):
                place_table(0, 0, k)
            place_dense(0, 0)
            read_table(0, NO - 1)
            act.wait_ge(table_read, NO)
            place_table(0, 0, NO - 1).then_inc(placed, 1)
            act.wait_ge(lo_made, NO)
            tile(0, 0)
            act.wait_ge(weights_loaded, 16 * 6)
            tile(0, 1)
            with act.Fori(0, QUARTERS - 1) as q:
                tile(q, 2, chunks_in(2))
                tile(q, 3, chunks_in(3))
                tile(q + 1, 0, between=lambda: mlp_layers(q, 0))
                tile(q + 1, 1, between=lambda: mlp_layers(q, 1))
            tile(QUARTERS - 1, 2)
            tile(QUARTERS - 1, 3)
            mlp_layers(QUARTERS - 1, 0)
            mlp_layers(QUARTERS - 1, 1)
            for t in range(2):
                act.wait_ge(idx_loaded[t], 16 * (QUARTERS + 1))

        @block.vector
        def _(dve):
            def compare(q, k, c):
                if c == 0:
                    dve.wait_ge(ids_spread, q * NO + k + 1)
                if not (isinstance(q, int) and q * NO + k == 0 and c < OH_BUFS):
                    dve.wait_ge(one_hot_used, CHUNKS * (q * NO + k) + c - OH_BUFS + 1)
                ids_at = spread_ids if first_quarter(q) else spread_bank[k % 2]
                dve.tensor_scalar(one_hot[:, (k * CHUNKS + c) % OH_BUFS, :], ids_at[0:CROWS, :], row_no[0:CROWS, c:c + 1],
                                  None, ALU.is_equal).then_inc(one_hot_made, 1)

            def split_low(k):
                dve.wait_ge(hi_made, k + 1)
                dve.tensor_tensor(tab_lo[0:CROWS, k].rearrange("p c d -> p (c d)"), raw[0:CROWS, k % RAW_BUFS, :],
                                  tab_hi[0:CROWS, k].rearrange("p c d -> p (c d)").bitcast(F32),
                                  ALU.subtract).then_inc(lo_made, 1)

            def read_unit(q, t, gu):
                u = len(T_UNITS) + gu
                dve.wait_ge(ring_filled, UNITS * (q * TILES + t) + u + 1)
                if gu == 0 and t % 2 == 0:
                    dve.wait_ge(z_stored[t // 2], Z_STORES * (q + 1))
                dve.tensor_copy(z_view(t, gu, 2), gram_view((UNITS * t + u) % 2, 2))
                dve.tensor_copy(z_view(t, gu, 3), gram_view((UNITS * t + u) % 2, 3)).then_inc(ring_read_dve, 1)

            def read_transposed(q, t):
                dve.wait_ge(ring_filled, UNITS * (q * TILES + t) + DVE_UNIT + 1)
                dve.tensor_copy(*transposed_unit(t, DVE_UNIT)).then_inc(ring_read_dve, 1)

            def tile(q, t, chunks=(), transposed=True):
                after = [chunks_due(len(chunks), (gu + 1) * G_PER_UNIT - 1) + 2 for gu in range(G_UNITS)]
                for n, chunk in enumerate(chunks):
                    compare(q + 1, *divmod(chunk, CHUNKS))
                    if n == DVE_AHEAD:
                        read_transposed(q, t)
                    if n in after:
                        read_unit(q, t, after.index(n))
                if transposed and not chunks:
                    read_transposed(q, t)
                for gu in range(G_UNITS):
                    if not chunks or after[gu] >= len(chunks):
                        read_unit(q, t, gu)

            dve.wait_ge(consts_made, 3)
            dve.tensor_copy(row_no[:], row_no_i[:]).then_inc(row_no_made, 1)
            dve.memset(one[:], 1.0).then_inc(row_no_made, 1)
            dve.wait_ge(row_no_made, 2)
            split_low(0)
            for k in range(NO):
                for c in range(CHUNKS):
                    if c not in ACT_CHUNKS:
                        compare(0, k, c)
                    elif c == ACT_CHUNKS[0] and k + 1 < NO:
                        split_low(k + 1)
                if k == T_AFTER:
                    read_transposed(0, 0)
                if k == 0:
                    dve.wait_ge(ids_converted, 1)
                    dve.memset(ct[:, :, :, :, NF:FPAD], 0.0).then_inc(padding_made, 1)
            tile(0, 0, transposed=False)
            tile(0, 1)
            with dve.Fori(0, QUARTERS - 1) as q:
                tile(q, 2, chunks_in(2))
                tile(q, 3, chunks_in(3))
                tile(q + 1, 0)
                tile(q + 1, 1)
            tile(QUARTERS - 1, 2)
            tile(QUARTERS - 1, 3)


def kernel(**inputs):
    import concourse.bacc as bacc
    from concourse.bass_utils import run_bass_kernel_spmd

    nc = bacc.Bacc("TRN2", target_bir_lowering=False, num_devices=1)
    ids = np.asarray(inputs["ids"])
    arrays = {name: np.asarray(inputs[name]) for name in
              ["W_top2"] + [f"tbl_{f}" for f in range(TABLES)]}
    arrays["ids"] = ids
    arrays["ids_rows"] = ids.T[ONE_HOT]
    arrays["dense_cols"] = np.asarray(inputs["r_dense_x"]).T
    arrays["W_top1"] = np.asarray(inputs["W_top1"])[pair_rows()]
    for name in ("b_top1", "b_top2", "W_top3"):
        arrays[name] = np.asarray(inputs[name]).reshape(-1, P).T
    feed, aps = {}, {}
    for name, a in arrays.items():
        a = np.ascontiguousarray(a)
        feed[f"in_{name}"] = a
        aps[name] = nc.dram_tensor(f"in_{name}", a.shape, mybir.dt.from_np(a.dtype), kind="ExternalInput").ap()
    out = nc.dram_tensor("out", (BATCH, 1), F32, kind="ExternalOutput").ap()
    dlrm(nc, aps["dense_cols"], aps["ids"], aps["ids_rows"], [aps[f"tbl_{f}"] for f in range(TABLES)],
         aps["W_top1"], aps["b_top1"], aps["W_top2"], aps["b_top2"], aps["W_top3"], out)
    return run_bass_kernel_spmd(nc, [feed], core_ids=[0]).results[0]["out"]
```
